# Optimizing a Trainium2 kernel written in Bass

```python
import numpy as np
import jax
import jax.numpy as jnp

def _softmax(x, axis=-1):
    return jax.nn.softmax(x, axis=axis)

def _gelu(x):
    return jax.nn.gelu(x, approximate=True)

def _silu(x):
    return jax.nn.silu(x)

def _sigmoid(x):
    return jax.nn.sigmoid(x)

def _layernorm(x, axis=-1, eps=1e-05):
    m = jnp.mean(x, axis=axis, keepdims=True)
    v = jnp.var(x, axis=axis, keepdims=True)
    return (x - m) / jnp.sqrt(v + eps)

def _scatter_add(tgt, idx, src, axis=0):
    return tgt.at[idx].add(src)

def _segment_sum(src, seg, n):
    return jax.ops.segment_sum(src, seg, n)
kernel_name = 'mk_gnn_preln_d1_gnn_r8_fece94'

def setup_inputs(seed: int=0):
    np.random.seed(seed)
    _w = jnp.asarray

    def _rec_inputs():
        import jax
        import jax.numpy as jnp
        _gk = jax.random.key(seed)
        x = -6.415e-05 + 1 * jax.random.normal(jax.random.fold_in(_gk, 1), (1250, 1024), jnp.float32)
        _s = jax.random.randint(jax.random.fold_in(_gk, 2), (20000,), 0, 1250, jnp.int32)
        _d = jax.random.randint(jax.random.fold_in(_gk, 3), (20000,), 0, 1250, jnp.int32)
        _loop = jnp.arange(1250, dtype=jnp.int32)
        src = jnp.concatenate([_s, _d, _loop])
        dst = jnp.concatenate([_d, _s, _loop])
        _o = jnp.argsort(dst, stable=True)
        src = src[_o]
        dst = dst[_o]
        return (x, src, dst)
    x, src, dst = _rec_inputs()

    def _L0_gnn_setup():
        import jax, jax.numpy as jnp
        import numpy as np
        N_NODES = 1250
        N_EDGES = 10000
        D = 1024

        def _sage_sum(h, src, dst, Ws, Wn, b):
            h_neigh = jax.ops.segment_sum(h[src], dst, num_segments=N_NODES)
            return h @ Ws + h_neigh @ Wn + b
        key = jax.random.key(seed)
        ks = jax.random.split(key, 8)
        s = 1.0 / np.sqrt(D)
        x = jax.random.normal(ks[0], (N_NODES, D), dtype=jnp.float32)
        edge_index = jax.random.randint(ks[1], (2, N_EDGES), 0, N_NODES, dtype=jnp.int32)
        Ws1 = jax.random.normal(ks[2], (D, D), dtype=jnp.float32) * s
        Wn1 = jax.random.normal(ks[3], (D, D), dtype=jnp.float32) * s
        b1 = jnp.zeros((D,), dtype=jnp.float32)
        Ws2 = jax.random.normal(ks[4], (D, D), dtype=jnp.float32) * s
        Wn2 = jax.random.normal(ks[5], (D, D), dtype=jnp.float32) * s
        b2 = jnp.zeros((D,), dtype=jnp.float32)
        return {'x': x, 'edge_index': edge_index, 'Ws1': Ws1, 'Wn1': Wn1, 'b1': b1, 'Ws2': Ws2, 'Wn2': Wn2, 'b2': b2}
    _L0_gnn_all = _L0_gnn_setup()
    _L0_gnn_in = {k: v for k, v in _L0_gnn_all.items() if k in ('Ws1', 'Wn1', 'b1', 'Ws2', 'Wn2', 'b2')}
    del _L0_gnn_all
    return {'x': x, 'src': src, 'dst': dst, 'L0_gnn_Ws1': _L0_gnn_in['Ws1'], 'L0_gnn_Wn1': _L0_gnn_in['Wn1'], 'L0_gnn_b1': _L0_gnn_in['b1'], 'L0_gnn_Ws2': _L0_gnn_in['Ws2'], 'L0_gnn_Wn2': _L0_gnn_in['Wn2'], 'L0_gnn_b2': _L0_gnn_in['b2']}

def reference(x, src, dst, L0_gnn_Ws1, L0_gnn_Wn1, L0_gnn_b1, L0_gnn_Ws2, L0_gnn_Wn2, L0_gnn_b2):
    import jax
    import jax.numpy as jnp

    def _L0_gnn_ref(x, edge_index, Ws1, Wn1, b1, Ws2, Wn2, b2):
        import jax, jax.numpy as jnp
        import numpy as np
        N_NODES = 1250
        N_EDGES = 10000
        D = 1024

        def _sage_sum(h, src, dst, Ws, Wn, b):
            h_neigh = jax.ops.segment_sum(h[src], dst, num_segments=N_NODES)
            return h @ Ws + h_neigh @ Wn + b
        src, dst = (edge_index[0], edge_index[1])
        h = _sage_sum(x, src, dst, Ws1, Wn1, b1)
        h = _sage_sum(h, src, dst, Ws2, Wn2, b2)
        return h
    edge_index = jnp.stack([src, dst])
    h = jnp.maximum(_layernorm(x, axis=-1), 0.0)
    x = x + _L0_gnn_ref(h, edge_index, L0_gnn_Ws1, L0_gnn_Wn1, L0_gnn_b1, L0_gnn_Ws2, L0_gnn_Wn2, L0_gnn_b2)
    return x

_drawn_inputs = setup_inputs


def setup_inputs(seed=0):
    import zlib

    import numpy as np

    out = dict(_drawn_inputs(seed))
    spreads = {'L0_gnn_b1': (0.0, 0.8), 'L0_gnn_b2': (0.0, 0.8)}
    factors = {}
    for name, (base, spread) in spreads.items():
        noise = np.random.default_rng([zlib.crc32(name.encode()), seed]).standard_normal(out[name].shape)
        drawn = base * np.exp(spread * noise) if base else spread * noise
        out[name] = jnp.asarray(drawn.astype(out[name].dtype))
    for name, factor in factors.items():
        out[name] = (out[name] * factor).astype(out[name].dtype)
    return out
```

```python
import concourse.bass as bass
from concourse import mybir
from contextlib import ExitStack

F32 = mybir.dt.float32
F32R = mybir.dt.float32r
F16 = mybir.dt.float16
I32 = mybir.dt.int32
ALU = mybir.AluOpType
ACT = mybir.ActivationFunctionType

P = 128
N = 1250
D = 1024
E = 41250
KF = D // P
NT = -(-N // P)
LAST = N - (NT - 1) * P
NPAD = NT * P
HALF = D // 2
HI, LO = 0, 1
PRODUCTS = ((HI, HI), (HI, LO), (LO, HI))
CH = ((0, 418), (418, 416), (834, 416))
WIN = 32
NW = NPAD // WIN
WPT = P // WIN
ROW = 10
EROWS = E // ROW
CAP = P * ROW
SAMPLE = 3
EP = 125
EPP = E // EP
RPP = EPP // ROW
NSAMP = RPP // SAMPLE
SLOTS = 8
EPS = 1e-5
EXACT = 4096
GROUPS = 6


def up(size):
    return -(-size // 32) * 32


def rows_of(t):
    return LAST if t == NT - 1 else P


def gnn_kernel(nc, x, src, dst, ws1, wn1, b1, ws2, wn2, b2, out):
    edge_rows = nc.dram_tensor("edge_rows", (EROWS + P + 3, 2 * ROW), F32, kind="Internal").ap()
    y1_dram = nc.dram_tensor("y1_dram", (N, D), F32, kind="Internal").ap()

    ctx = ExitStack()
    with ctx:
        base = up(nc.sbuf_base)

        def at(name, shape, dt, offset):
            return nc.alloc_sbuf_tensor_at(name, shape, dt, offset=base + offset)

        def sem(name):
            return ctx.enter_context(nc.semaphore(name))

        AT0 = 2 * KF * N * 4
        R0 = AT0 + NT * NPAD * 4
        W0 = R0 + 2 * HALF * 4 * NT
        HT = at("HT", [P, 2, KF, N], F32R, 0)
        AT = at("AT", [P, NT, NPAD], F32R, AT0)
        xin = at("xin", [P, NT, D], F32, AT0)
        hbuf = at("hbuf", [P, 2, D], F32, AT0 + NT * D * 4)
        W = at("W", [P, KF, 2, HALF], F32R, W0)
        W_raw = at("W_raw", [P, KF, 2, HALF], F32, W0)
        o = R0
        onehot_src = at("onehot_src", [P, SLOTS, N], F16, o); o += up(SLOTS * N * 2)
        iota_f16 = at("iota_f16", [P, N], F16, o); o += up(N * 2)
        DST0 = o
        onehot_dst = at("onehot_dst", [P, WPT * ROW, WIN], F16, o); o += up(WPT * ROW * WIN * 2)
        window_edges = at("window_edges", [P, NW, 2 * ROW], F32, o); o += up(NW * 2 * ROW * 4)
        A_rows = at("A_rows", [P, N], F32, o); o += up(N * 4)
        A_cols = at("A_cols", [P, NT, P], F32, o); o += up(NT * P * 4)
        ident = at("ident", [P, P], F32, o); o += up(P * 4)
        assert o <= W0, o - W0
        o = W0 + KF * 2 * HALF * 4
        y1_out = at("y1_out", [P, 2, HALF], F32, o); o += up(2 * HALF * 4)
        edges = at("edges", [EP, RPP, 2, ROW], F32, o); o += up(EPP * 2 * 4)
        C0 = o
        edge_ints = at("edge_ints", [EP, 2, EPP], I32, R0)
        pad_row = at("pad_row", [P, 2 * ROW], F32, R0 + up(2 * EPP * 4))
        h1T = at("h1T", [P, KF, N], F32, R0)
        ST0 = W0 + 5 * 2 * HALF * 4
        W_st = at("W_st", [P, 2, KF, P], F32R, ST0)
        W_st_raw = at("W_st_raw", [P, 2, KF, P], F32, ST0)
        y_st = at("y_st", [P, 2, NT, P], F32R, ST0 + 2 * D * 4)
        y_st_raw = at("y_st_raw", [P, 2, NT, P], F32, ST0 + 2 * D * 4)
        y2 = at("y2", [P, NT, 2, HALF], F32R, R0)
        x_out = at("x_out", [P, 2, HALF], F32, W0 + KF * 2 * HALF * 4)
        b2_sb = at("b2_sb", [P, HALF], F32, W0 + KF * 2 * HALF * 4 + 2 * HALF * 4)
        o = max(C0, ST0 + 2 * D * 4 + 2 * NPAD * 4)
        b1_sb = at("b1_sb", [P, KF], F32, o); o += up(KF * 4)
        stats = at("stats", [P, 2, 6], F32, o); o += 64
        mv = at("mv", [P, 2, 2], F32, o); o += 32
        iota32 = at("iota32", [P, WIN], F32, o); o += up(WIN * 4)
        degree = at("degree", [P, NT], F32, o); o += 64
        check = at("check", [P, 2], F32, o); o += 32
        ones = at("ones", [P, 1], F32, o); o += 32
        unused = at("unused", [P, 8], F32, o); o += 32
        minus_half = at("minus_half", [P, 1], F32, o); o += 32
        flags_f = at("flags_f", [P, 4], F32, o); o += 32
        flags = at("flags", [1, 2], I32, o); o += 32
        early = AT0 + (NT + 2) * D * 4
        samples = at("samples", [EP, NW], F32, early)
        row_f = at("row_f", [1, NW], F32, early + NW * 4)
        row_i = at("row_i", [1, NW], I32, early + 2 * NW * 4)
        win_start = at("win_start", [P, NW], F32, early + 3 * NW * 4)
        any_dst = at("any_dst", [P, 2, P], F16, DST0)
        zeros = at("zeros", [P, P], F16, DST0 + 2 * P * 2)
        assert base + o <= nc.sbuf_usable_end, (base + o, nc.sbuf_usable_end)

        PS = ctx.enter_context(nc.psum_tensor("PS", [P, 8, 512], F32))
        PSF = PS[:, :, :].rearrange("p b n -> p (b n)")

        x_in = sem("x_in"); edges_in = sem("edges_in"); consts_in = sem("consts_in"); b2_in = sem("b2_in")
        x_in_t = [sem(f"x_in_{t}") for t in range(NT)]
        setup = sem("setup"); pool_self = sem("pool_self"); dve_self = sem("dve_self"); act_self = sem("act_self")
        edges_cast = sem("edges_cast"); rows_saved = sem("rows_saved"); sampled = sem("sampled")
        counted = sem("counted"); row_found = sem("row_found"); windows_in = sem("windows_in")
        var_ready = sem("var_ready"); eps_added = sem("eps_added"); rstd_ready = sem("rstd_ready"); h_ready = sem("h_ready"); h_turned = sem("h_turned"); ht_hi = sem("ht_hi"); ht_lo = sem("ht_lo")
        w_raw = [sem(f"w_raw_{k}") for k in range(KF)]
        w_hi = sem("w_hi"); w_lo = sem("w_lo"); w_used = sem("w_used")
        dst_ready = sem("dst_ready")
        src_ready = sem("src_ready"); src_free = sem("src_free")
        counts_saved = sem("counts_saved")
        turned = sem("turned"); cols_ready = sem("cols_ready"); at_written = sem("at_written")
        y1_done = sem("y1_done"); y1_freed = sem("y1_freed"); y1_saved = [sem(f"y1_saved_{i}") for i in range(2)]
        check_ready = sem("check_ready"); check_summed = sem("check_summed"); flags_ready = sem("flags_ready")
        g_ready = sem("g_ready"); g_free = sem("g_free"); g_counts = sem("g_counts"); g_saved = sem("g_saved")
        g_turned = sem("g_turned"); g_cols = sem("g_cols"); g_written = sem("g_written"); g_self = sem("g_self")
        wst_in = sem("wst_in"); wst_hi = sem("wst_hi"); wst_lo = sem("wst_lo"); wst_used = sem("wst_used")
        yst_in = sem("yst_in"); yst_hi = sem("yst_hi"); yst_lo = sem("yst_lo")
        h1_done = sem("h1_done"); h1_freed = sem("h1_freed"); h1_hi = sem("h1_hi"); h1_lo = sem("h1_lo")
        tile_done = sem("tile_done"); y2_hi = sem("y2_hi"); tile_freed = sem("tile_freed")
        x2_in = [sem(f"x2_in_{i}") for i in range(2)]; x2_biased = sem("x2_biased")
        out_saved = [sem(f"out_saved_{i}") for i in range(2)]

        RING34 = (6, 7, 0, 1)
        BR1, Y1_BANKS = 3, 5
        ACH = ((0, 512), (512, 512), (1024, N - 1024))
        CHBANK = ((0, 1, 2), (3, 4, 5))

        block = ctx.enter_context(nc.Block())

        @block.sync
        def _(sp):
            sp.dma_start(edge_ints[:, 0, :], src.rearrange("(p e) -> p e", p=EP)).then_inc(edges_in, 16)
            sp.dma_start(edge_ints[:, 1, :], dst.rearrange("(p e) -> p e", p=EP)).then_inc(edges_in, 16)
            for t in range(NT):
                r = rows_of(t)
                sp.dma_start(xin[:r, t, :], x[t * P:t * P + r, :]).then_inc(x_in_t[t], 16)
            with nc.allow_non_contiguous_dma("4 KB bias as a column for each feature tile"):
                sp.dma_start(b1_sb[:, :], b1.rearrange("(k p) -> p k", p=P)).then_inc(consts_in, 16)

            sp.wait_ge(edges_cast, 2)
            sp.dma_start(edge_rows[0:EROWS, :].rearrange("(p r) c -> p (r c)", p=EP),
                         edges[:, :, :, :].rearrange("p r a c -> p (r a c)")).then_inc(rows_saved, 16)
            sp.wait_ge(setup, 1)
            sp.dma_start(edge_rows[EROWS:EROWS + P, :], pad_row[:, :]).then_inc(rows_saved, 16)

            def slab_used(use, k):
                if k == KF - 1 and use < 2:
                    sp.wait_ge(y1_done, (use + 1) * NT)
                elif k == KF - 1 and use % 2 == 0:
                    sp.wait_ge(tile_done, use // 2 * 2 * NT - NT)
                else:
                    sp.wait_ge(w_used, sum((KF - 1, KF - 1, KF - 1, KF, KF - 1, KF)[:use]) + k + 1)

            def load_w(m, half, k):
                sp.dma_start(W_raw[:, k, LO, :],
                             m[k * P:(k + 1) * P, half * HALF:(half + 1) * HALF]).then_inc(w_raw[k], 16)

            for k in range(KF):
                load_w(wn1, 0, k)

            sp.wait_ge(rows_saved, 32)
            sp.wait_ge(row_found, 1)
            with sp.Fori(0, NW) as w:
                r = sp.value_load(row_i[0:1, bass.ds(w, 1)], min_val=0, max_val=EROWS)
                sp.dma_start(window_edges[:, bass.ds(w, 1), :],
                             edge_rows[bass.ds(r, P), :].unsqueeze(1)).then_inc(windows_in, 16)

            for half in range(2):
                for a in range(NT // 2):
                    n = half * (NT // 2) + a
                    for t in (2 * a, 2 * a + 1):
                        if half == 0 and t == NT - 1:
                            for k in range(KF):
                                slab_used(0, k)
                                load_w(wn1, 1, k)
                        r = rows_of(t)
                        sp.wait_ge(y1_freed, Y1_BANKS + half * NT + t + 1)
                        sp.dma_start(y1_dram[t * P:t * P + r, half * HALF:(half + 1) * HALF],
                                     y1_out[:r, t % 2, :]).then_inc(y1_saved[t % 2], 16)
                    sp.wait_ge(cols_ready, 2 * (n + 1) + 1)
                    sp.dma_start(AT[:, 0:NT - 1, n * P:(n + 1) * P].bitcast(F32), A_cols[:, 0:NT - 1, :]).then_inc(at_written, 16)
                    sp.dma_start(AT[:LAST, NT - 1, n * P:(n + 1) * P].bitcast(F32), A_cols[:LAST, NT - 1, :]).then_inc(at_written, 16)

            sp.wait_ge(flags_ready, 1)
            redo = sp.value_load(flags[0:1, 0:1], min_val=0, max_val=1)
            with sp.If(redo != 0):
                sp.wait_ge(at_written, NT * 32)
                for t in range(NT):
                    sp.wait_ge(g_cols, 2 * t + 3)
                    sp.dma_start(AT[:, 0:NT - 1, t * P:(t + 1) * P].bitcast(F32), A_cols[:, 0:NT - 1, :]).then_inc(g_written, 16)
                    sp.dma_start(AT[:LAST, NT - 1, t * P:(t + 1) * P].bitcast(F32), A_cols[:LAST, NT - 1, :]).then_inc(g_written, 16)
                    sp.wait_ge(g_written, 32 * t + 32)

            slab_used(1, KF - 1)
            for j in range(KF):
                if j:
                    sp.wait_ge(wst_used, j)
                sp.dma_start(W_st_raw[:, LO, :, :],
                             ws1[:, j * P:(j + 1) * P].rearrange("(k p) c -> p k c", p=P)).then_inc(wst_in, 16)
                sp.wait_ge(y1_saved[0], NT * 16)
                sp.wait_ge(y1_saved[1], NT * 16)
                if j:
                    sp.wait_ge(h1_done, j)
                sp.dma_start(y_st_raw[:, LO, 0:NT - 1, :],
                             y1_dram[0:(NT - 1) * P, j * P:(j + 1) * P].rearrange("(s p) c -> p s c", p=P)).then_inc(yst_in, 16)
                sp.dma_start(y_st_raw[:LAST, LO, NT - 1, :],
                             y1_dram[(NT - 1) * P:N, j * P:(j + 1) * P]).then_inc(yst_in, 16)

            sp.wait_ge(h1_done, KF - 1)
            for k in range(KF):
                if k == 5:
                    sp.wait_ge(wst_used, KF)
                if k == 7:
                    sp.wait_ge(h1_done, KF)
                load_w(wn2, 0, k)

            def load_x(t, half, r, n):
                if n >= 2:
                    sp.wait_ge(out_saved[n % 2], 16 * (n // 2))
                sp.dma_start(x_out[:r, n % 2, :],
                             x[t * P:t * P + r, half * HALF:(half + 1) * HALF]).then_inc(x2_in[n % 2], 16)

            for half in range(2):
                if half:
                    sp.wait_ge(x2_biased, NT)
                else:
                    sp.wait_ge(h1_done, KF)
                sp.dma_start(b2_sb[:, :], b2[half * HALF:(half + 1) * HALF].partition_broadcast(P)).then_inc(b2_in, 16)
                for k in range(KF):
                    slab_used(2 + 2 * half, k)
                    load_w(ws2, half, k)
                for t in range(NT):
                    n = half * NT + t
                    load_x(t, half, rows_of(t), n)
                    if t == NT - 1 and half == 0:
                        for k in range(KF):
                            slab_used(3, k)
                            load_w(wn2, 1, k)
                    if t:
                        r = rows_of(t - 1)
                        sp.wait_ge(tile_freed, 4 + 2 * NT * half + NT + t)
                        sp.dma_start(out[(t - 1) * P:(t - 1) * P + r, half * HALF:(half + 1) * HALF],
                                     x_out[:r, (n - 1) % 2, :]).then_inc(out_saved[(n - 1) % 2], 16)
                sp.wait_ge(tile_freed, 4 + 2 * NT * (half + 1))
                sp.dma_start(out[(NT - 1) * P:N, half * HALF:(half + 1) * HALF],
                             x_out[:LAST, (NT - 1) % 2, :]).then_inc(out_saved[(NT - 1) % 2], 16)
            for i in range(2):
                sp.wait_ge(out_saved[i], NT * 16)

        @block.gpsimd
        def _(pool):
            nc.gpsimd.memset(pad_row[:, :], -1.0).then_inc(setup, 1)
            nc.gpsimd.iota(win_start[:, :], pattern=[[WIN, NW]], base=0, channel_multiplier=0,
                           allow_small_or_imprecise_dtypes=True).then_inc(setup, 1)
            nc.gpsimd.memset(unused[:, 0:1], 0.0).then_inc(cols_ready, 1)
            nc.gpsimd.memset(unused[:, 1:2], 0.0).then_inc(g_cols, 1)
            nc.gpsimd.memset(unused[:, 2:3], 0.0).then_inc(y1_freed, Y1_BANKS)
            nc.gpsimd.memset(unused[:, 3:4], 0.0).then_inc(h1_freed, 3 + 1)
            nc.gpsimd.memset(unused[:, 4:5], 0.0).then_inc(tile_freed, 4)
            nc.gpsimd.memset(ident[:, :], 0.0).then_inc(pool_self, 1)
            pool.wait_ge(pool_self, 1)
            nc.gpsimd.affine_select(out=ident[:, :], in_=ident[:, :], compare_op=ALU.not_equal, fill=1.0,
                                    base=0, pattern=[[-1, P]], channel_multiplier=1).then_inc(setup, 1)
            nc.gpsimd.memset(ones[:, :], 1.0).then_inc(setup, 1)
            nc.gpsimd.memset(minus_half[:, :], -0.5).then_inc(pool_self, 1)
            pool.wait_ge(pool_self, 2)
            nc.gpsimd.iota(iota32[:, :], pattern=[[1, WIN]], base=0, channel_multiplier=0,
                           allow_small_or_imprecise_dtypes=True).then_inc(pool_self, 1)
            nc.gpsimd.iota(iota_f16[:, :], pattern=[[1, N]], base=0, channel_multiplier=0,
                           allow_small_or_imprecise_dtypes=True).then_inc(src_free, SLOTS)

            for t in range(NT):
                r = rows_of(t)
                pool.wait_ge(var_ready, t + 1)
                nc.gpsimd.tensor_scalar(mv[:r, t % 2, 1:2], mv[:r, t % 2, 1:2], EPS, None, ALU.add).then_inc(eps_added, 1)
                pool.wait_ge(eps_added, t + 1)
                nc.gpsimd.tensor_tensor(mv[:r, t % 2, 1:2], mv[:r, t % 2, 1:2], minus_half[:r, :], ALU.pow).then_inc(rstd_ready, 1)

            def w_low(n, k):
                pool.wait_ge(w_hi, n + 1)
                nc.gpsimd.tensor_tensor(W[:, k, LO, :], W_raw[:, k, LO, :], W[:, k, HI, :].bitcast(F32),
                                        ALU.subtract).then_inc(w_lo, 1)

            for k in range(KF):
                w_low(k, k)

            pool.wait_ge(windows_in, NW * 16)
            nc.gpsimd.tensor_tensor(window_edges[:, :, ROW:], window_edges[:, :, ROW:],
                                    win_start[:, :].unsqueeze(2).to_broadcast([P, NW, ROW]),
                                    ALU.subtract).then_inc(pool_self, 1)
            pool.wait_ge(pool_self, 4)
            for k in range(KF):
                w_low(KF + k, k)

            for k in range(KF):
                w_low(2 * KF + k, k)
            n = 3 * KF
            for half in range(2):
                for k in range(KF):
                    w_low(n, k)
                    n += 1
                pool.wait_ge(b2_in, 16 * (half + 1))
                for t in range(NT):
                    i, r = half * NT + t, rows_of(t)
                    pool.wait_ge(x2_in[i % 2], 16 * (i // 2 + 1))
                    nc.gpsimd.tensor_tensor(x_out[:r, i % 2, :], x_out[:r, i % 2, :], b2_sb[:r, :],
                                            ALU.add).then_inc(x2_biased, 1)
                if half == 0:
                    for k in range(KF):
                        w_low(n, k)
                        n += 1

        @block.scalar
        def _(act):
            def w_high(n, k):
                act.wait_ge(w_raw[k], 16 * (n // KF + 1))
                nc.scalar.activation(W[:, k, HI, :], W_raw[:, k, LO, :], ACT.Copy).then_inc(w_hi, 1)

            for k in range(4):
                w_high(k, k)
            for t in range(NT):
                r = rows_of(t)
                b = 2 * (t % 2)
                act.wait_ge(h_turned, t + 1)
                nc.scalar.activation(HT[:, HI, :, t * P:t * P + r],
                                     PSF[:, b * 512:b * 512 + D].rearrange("p (k c) -> p k c", k=KF)[:, :, 0:r],
                                     ACT.Relu).then_inc(ht_hi, 1)
            for k in range(4, KF):
                w_high(k, k)

            for half in range(2):
                for a in range(NT // 2):
                    n = half * (NT // 2) + a
                    for t in (2 * a, 2 * a + 1):
                        if half == 0 and t == NT - 1:
                            for k in range(KF):
                                w_high(KF + k, k)
                        if t == 2 * a + 1:
                            act.wait_ge(src_free, SLOTS + (n + 1) * WPT * ROW)
                            if n:
                                act.wait_ge(turned, n)
                            nc.scalar.activation(A_rows[:, :], PSF[:, 0:N], ACT.Copy,
                                                 accum_out=degree[:, n:n + 1]).then_inc(counts_saved, 1)
                        r = rows_of(t)
                        i = half * NT + t
                        act.wait_ge(y1_done, i + 1)
                        if i >= 2:
                            act.wait_ge(y1_saved[i % 2], 16 * (i // 2))
                        nc.scalar.activation(y1_out[:r, i % 2, :], PS[:r, BR1 + i % 5, :], ACT.Copy).then_inc(y1_freed, 1)
                    act.wait_ge(turned, n + 1)
                    if n:
                        act.wait_ge(at_written, 32 * n)
                    nc.scalar.activation(A_cols[:, 0:NT - 1, :],
                                         PSF[:, 0:(NT - 1) * P].rearrange("p (s c) -> p s c", s=NT - 1), ACT.Copy).then_inc(cols_ready, 1)
                    nc.scalar.activation(A_cols[:LAST, NT - 1, :], PSF[:LAST, (NT - 1) * P:NT * P], ACT.Copy).then_inc(cols_ready, 1)

            act.wait_ge(flags_ready, 1)
            redo = act.value_load(flags[0:1, 0:1], min_val=0, max_val=1)
            with act.If(redo != 0):
                act.wait_ge(at_written, 32 * NT)
                for t in range(NT):
                    act.wait_ge(g_counts, t + 1)
                    nc.scalar.activation(A_rows[:, :], PSF[:, 0:N], ACT.Copy).then_inc(g_saved, 1)
                    act.wait_ge(g_turned, t + 1)
                    if t:
                        act.wait_ge(g_written, 32 * t)
                    nc.scalar.activation(A_cols[:, 0:NT - 1, :],
                                         PSF[:, 0:(NT - 1) * P].rearrange("p (s c) -> p s c", s=NT - 1), ACT.Copy).then_inc(g_cols, 1)
                    nc.scalar.activation(A_cols[:LAST, NT - 1, :], PSF[:LAST, (NT - 1) * P:NT * P], ACT.Copy).then_inc(g_cols, 1)
                act.wait_ge(g_written, 32 * NT)

            def stationary_high(j):
                act.wait_ge(wst_in, 16 * j + 16)
                nc.scalar.activation(W_st[:, HI, :, :], W_st_raw[:, LO, :, :], ACT.Copy).then_inc(wst_hi, 1)
                act.wait_ge(yst_in, 32 * j + 32)
                nc.scalar.activation(y_st[:, HI, 0:NT - 1, :], y_st_raw[:, LO, 0:NT - 1, :], ACT.Copy).then_inc(yst_hi, 1)
                nc.scalar.activation(y_st[:LAST, HI, NT - 1, :], y_st_raw[:LAST, LO, NT - 1, :], ACT.Copy).then_inc(yst_hi, 1)

            def h1_save(j, parity):
                act.wait_ge(h1_done, j + 1)
                for c, (o_, w_) in enumerate(CH):
                    nc.scalar.activation(h1T[:, bass.ds(j, 1), o_:o_ + w_], PS[:, CHBANK[parity][c], 0:w_].unsqueeze(1),
                                         ACT.Identity, bias=b1_sb[:, bass.ds(j, 1)]).then_inc(h1_freed, 1)

            act.wait_ge(consts_in, 16)
            act.wait_ge(y1_saved[0], NT * 16)
            act.wait_ge(y1_saved[1], NT * 16)
            act.wait_ge(at_written, 32 * NT)
            stationary_high(0)
            with act.Fori(0, KF // 2 - 1) as q:
                for parity in range(2):
                    stationary_high(2 * q + parity + 1)
                    h1_save(2 * q + parity, parity)
            stationary_high(KF - 1)
            h1_save(KF - 2, 0)
            act.wait_ge(wst_used, KF)
            act.wait_ge(h1_freed, 1 + 3 * KF)
            for k in range(KF - 1):
                nc.scalar.activation(HT[:, HI, k, :], h1T[:, k, :], ACT.Copy).then_inc(h1_hi, 1)
            for k in range(5):
                w_high(2 * KF + k, k)
            act.wait_ge(h1_done, KF)
            for c, (o_, w_) in enumerate(CH):
                nc.scalar.activation(HT[:, HI, KF - 1, o_:o_ + w_], PS[:, CHBANK[1][c], 0:w_],
                                     ACT.Identity, bias=b1_sb[:, KF - 1:KF]).then_inc(h1_hi, 1)
            for k in range(5, KF):
                w_high(2 * KF + k, k)

            n = 3 * KF
            for half in range(2):
                for t in range(NT):
                    if t == NT - 1:
                        for k in range(KF):
                            w_high(n, k)
                            n += 1
                    r, i = rows_of(t), 2 * NT * half + t
                    act.wait_ge(tile_done, i + 1)
                    nc.scalar.activation(y2[:r, t, HI, :], PS[:r, RING34[i % 4], :], ACT.Copy).then_inc(y2_hi, 1)
                if half == 0:
                    for k in range(KF):
                        w_high(n, k)
                        n += 1

        @block.vector
        def _(dve):
            count = [0]

            def chain(ins):
                ins.then_inc(dve_self, 1)
                count[0] += 1
                dve.wait_ge(dve_self, count[0])

            dve.wait_ge(edges_in, 32)
            for a in range(2):
                nc.vector.tensor_copy(edges[:, :, a, :], edge_ints[:, a, :].rearrange("p (r c) -> p r c", c=ROW)).then_inc(edges_cast, 1)
            dve.wait_ge(edges_cast, 2)
            dve.wait_ge(setup, 2)
            for q in range(NSAMP):
                s = edges[:, SAMPLE * q, 1, 0:1]
                if q == 0:
                    chain(nc.vector.tensor_scalar(samples[:, :], win_start[:EP, :], s, None, ALU.is_gt))
                else:
                    ins = nc.vector.scalar_tensor_tensor(samples[:, :], win_start[:EP, :], s, samples[:, :], ALU.is_gt, ALU.add)
                    if q < NSAMP - 1:
                        chain(ins)
                    else:
                        ins.then_inc(sampled, 1)
            dve.wait_ge(counted, 1)
            chain(nc.vector.tensor_scalar(row_f[:, :], PS[0:1, 7, 0:NW], float(SAMPLE), float(-SAMPLE), ALU.mult, ALU.add))
            chain(nc.vector.tensor_scalar(row_f[:, :], row_f[:, :], 0.0, None, ALU.max))
            nc.vector.tensor_copy(row_i[:, :], row_f[:, :]).then_inc(row_found, 1)

            def low_of_h(t):
                r = rows_of(t)
                b = 2 * (t % 2)
                dve.wait_ge(ht_hi, t + 1)
                nc.vector.scalar_tensor_tensor(
                    HT[:, LO, :, t * P:t * P + r],
                    PSF[:, b * 512:b * 512 + D].rearrange("p (k c) -> p k c", k=KF)[:, :, 0:r], 0.0,
                    HT[:, HI, :, t * P:t * P + r].bitcast(F32), ALU.max, ALU.subtract).then_inc(ht_lo, 1)

            for t in range(NT):
                r = rows_of(t)
                dve.wait_ge(x_in_t[t], 16)
                nc.vector.bn_stats(stats[:r, 0, :], xin[:r, t, 0:HALF])
                chain(nc.vector.bn_stats(stats[:r, 1, :], xin[:r, t, HALF:D]))
                nc.vector.bn_aggr(mv[:r, t % 2, :], stats[:r, :, :].rearrange("p a b -> p (a b)")).then_inc(var_ready, 1)
                dve.wait_ge(rstd_ready, t + 1)
                if t >= 2:
                    dve.wait_ge(h_turned, t - 1)
                nc.vector.tensor_scalar(hbuf[:r, t % 2, :], xin[:r, t, :], mv[:r, t % 2, 0:1], mv[:r, t % 2, 1:2],
                                        ALU.subtract, ALU.mult).then_inc(h_ready, 1)
                if t:
                    low_of_h(t - 1)
            low_of_h(NT - 1)

            dve.wait_ge(pool_self, 4)
            with dve.Fori(0, NT) as a:
                dve.wait_ge(src_free, a * (WPT * ROW) + SLOTS)
                nc.vector.tensor_tensor(
                    onehot_dst[:, :, :].rearrange("p (w i) m -> p w i m", w=WPT),
                    window_edges[:, bass.ds(a * WPT, WPT), ROW:].unsqueeze(3).to_broadcast([P, WPT, ROW, WIN]),
                    iota32[:, :].unsqueeze(1).unsqueeze(1).to_broadcast([P, WPT, ROW, WIN]),
                    ALU.is_equal).then_inc(dst_ready, 1)
                for i in range(ROW):
                    for j in range(WPT):
                        q = i * WPT + j
                        dve.wait_ge(src_free, a * (WPT * ROW) + q + 1)
                        nc.vector.tensor_scalar(onehot_src[:, q % SLOTS, :], iota_f16[:, :],
                                                window_edges[:, bass.ds(a * WPT + j, 1), i], None,
                                                ALU.is_equal).then_inc(src_ready, 1)

            dve.wait_ge(counts_saved, NT)
            nc.vector.reduce_sum(check[:, 0:1], degree[:, :], axis=mybir.AxisListType.X)
            chain(nc.vector.reduce_max(check[:, 1:2], degree[:, :], axis=mybir.AxisListType.X))
            nc.vector.tensor_scalar(check[:, 1:2], check[:, 1:2], float(EXACT), None, ALU.is_gt).then_inc(check_ready, 1)
            dve.wait_ge(check_summed, 1)
            nc.vector.tensor_scalar(flags_f[0:1, 0:1], PS[0:1, BR1, 0:1], float(E), None, ALU.not_equal)
            chain(nc.vector.tensor_scalar(flags_f[0:1, 1:2], PS[0:1, BR1, 1:2], 0.0, None, ALU.is_gt))
            chain(nc.vector.tensor_tensor(flags_f[0:1, 1:2], flags_f[0:1, 0:1], flags_f[0:1, 1:2], ALU.max))
            nc.vector.tensor_copy(flags[0:1, :], flags_f[0:1, 0:2]).then_inc(flags_ready, 1)

            dve.wait_ge(flags_ready, 1)
            redo = dve.value_load(flags[0:1, 0:1], min_val=0, max_val=1)
            with dve.If(redo != 0):
                nc.vector.memset(zeros[:, :], 0.0).then_inc(g_free, 2)
                with dve.Fori(0, NT) as t:
                    with dve.Fori(0, RPP) as r:
                        for q in range(ROW):
                            dve.wait_ge(g_free, t * EPP + r * ROW + (q + 1))
                            nc.vector.tensor_scalar(onehot_src[:EP, q % 2, :], iota_f16[:EP, :],
                                                    edges[:, bass.ds(r, 1), 0, q], None, ALU.is_equal)
                            nc.vector.tensor_scalar(any_dst[:EP, q % 2, :], iota_f16[:EP, 0:P],
                                                    edges[:, bass.ds(r, 1), 1, q], None, ALU.is_equal).then_inc(g_ready, 1)
                    nc.vector.tensor_scalar(edges[:, :, 1, :], edges[:, :, 1, :], float(P), None, ALU.subtract).then_inc(g_self, 1)
                    dve.wait_ge(g_self, t + 1)

            with dve.Fori(0, KF) as j:
                dve.wait_ge(wst_hi, j + 1)
                nc.vector.tensor_tensor(W_st[:, LO, :, :], W_st_raw[:, LO, :, :], W_st[:, HI, :, :].bitcast(F32),
                                        ALU.subtract).then_inc(wst_lo, 1)
                dve.wait_ge(yst_hi, 2 * j + 2)
                nc.vector.tensor_tensor(y_st[:, LO, 0:NT - 1, :], y_st_raw[:, LO, 0:NT - 1, :],
                                        y_st[:, HI, 0:NT - 1, :].bitcast(F32), ALU.subtract).then_inc(yst_lo, 1)
                nc.vector.tensor_tensor(y_st[:LAST, LO, NT - 1, :], y_st_raw[:LAST, LO, NT - 1, :],
                                        y_st[:LAST, HI, NT - 1, :].bitcast(F32), ALU.subtract).then_inc(yst_lo, 1)
            for k in range(KF - 1):
                dve.wait_ge(h1_hi, k + 1)
                nc.vector.tensor_tensor(HT[:, LO, k, :], h1T[:, k, :], HT[:, HI, k, :].bitcast(F32),
                                        ALU.subtract).then_inc(h1_lo, 1)
            for c, (o_, w_) in enumerate(CH):
                dve.wait_ge(h1_hi, KF + c)
                nc.vector.scalar_tensor_tensor(HT[:, LO, KF - 1, o_:o_ + w_], PS[:, CHBANK[1][c], 0:w_],
                                               b1_sb[:, KF - 1:KF], HT[:, HI, KF - 1, o_:o_ + w_].bitcast(F32),
                                               ALU.add, ALU.subtract).then_inc(h1_lo, 1)

            for half in range(2):
                for t in range(NT):
                    r, n = rows_of(t), 2 * NT * half + t
                    dve.wait_ge(y2_hi, NT * half + t + 1)
                    nc.vector.tensor_tensor(y2[:r, t, LO, :], PS[:r, RING34[n % 4], :], y2[:r, t, HI, :].bitcast(F32),
                                            ALU.subtract).then_inc(tile_freed, 1)
                for t in range(NT):
                    r, n = rows_of(t), 2 * NT * half + NT + t
                    dve.wait_ge(x2_biased, NT * half + t + 1)
                    dve.wait_ge(tile_done, n + 1)
                    i = (NT * half + t) % 2
                    nc.vector.tensor_tensor(x_out[:r, i, :], PS[:r, RING34[n % 4], :], x_out[:r, i, :],
                                            ALU.add).then_inc(tile_freed, 1)

        @block.tensor
        def _(pe):
            def turn_counts(saved, saved_n, done):
                pe.wait_ge(saved, saved_n)
                for s in range(NT):
                    r = rows_of(s)
                    last = nc.tensor.transpose(PSF[:r, s * P:(s + 1) * P], A_rows[:, s * P:s * P + r], ident[:, :])
                last.then_inc(done, 1)

            pe.wait_ge(setup, 4)
            pe.wait_ge(sampled, 1)
            nc.tensor.matmul(PS[0:1, 7, 0:NW], ones[:EP, :], samples[:, :], start=True, stop=True).then_inc(counted, 1)

            for t in range(NT):
                r = rows_of(t)
                pe.wait_ge(h_ready, t + 1)
                if t >= 2:
                    pe.wait_ge(ht_lo, t - 1)
                for k in range(KF):
                    c = 2 * (t % 2) * 512 + k * P
                    last = nc.tensor.transpose(PSF[:, c:c + r], hbuf[:r, t % 2, k * P:(k + 1) * P], ident[:r, :r])
                last.then_inc(h_turned, 1)
            pe.wait_ge(ht_lo, NT)
            pe.wait_ge(row_found, 1)

            def slab_products(bank, t, k, first, last):
                r = rows_of(t)
                for m, (a, b) in enumerate(PRODUCTS):
                    ins = nc.tensor.matmul(PS[:r, bank, :], HT[:, a, k, t * P:t * P + r], W[:, k, b, :],
                                           start=first and m == 0, stop=last and m == 2)
                return ins

            with pe.Fori(0, 2) as half:
                for a in range(NT // 2):
                    n = half * (NT // 2) + a
                    work = [(t, k) for t in (2 * a, 2 * a + 1) for k in range(KF)]
                    bounds = [len(work) * g // GROUPS for g in range(GROUPS + 1)]
                    for g in range(GROUPS):
                        for t, k in work[bounds[g]:bounds[g + 1]]:
                            if k == 0:
                                pe.wait_ge(y1_freed, half * NT + (t + 1))
                            if t == 0:
                                pe.wait_ge(w_lo, half * KF + (k + 1))
                            ins = slab_products(BR1 + t % 5, t, k, k == 0, k == KF - 1)
                            if k == KF - 1:
                                ins.then_inc(y1_done, 1)
                            elif t == NT - 1:
                                ins.then_inc(w_used, 1)
                        if g == GROUPS - 1:
                            continue
                        if g == 0:
                            pe.wait_ge(dst_ready, n + 1)
                            pe.wait_ge(cols_ready, n * 2 + 1)
                        for i in range(g * ROW // (GROUPS - 1), (g + 1) * ROW // (GROUPS - 1)):
                            pe.wait_ge(src_ready, n * (WPT * ROW) + (i + 1) * WPT)
                            for c, (o_, w_) in enumerate(ACH):
                                for j in range(WPT):
                                    ins = nc.tensor.matmul(PS[j * WIN:(j + 1) * WIN, c, 0:w_],
                                                           onehot_dst[:, j * ROW + i, :],
                                                           onehot_src[:, (i * WPT + j) % SLOTS, o_:o_ + w_],
                                                           start=i == 0, stop=i == ROW - 1)
                            ins.then_inc(src_free, WPT)
                    turn_counts(counts_saved, n + 1, turned)

            pe.wait_ge(y1_freed, Y1_BANKS + 2 * NT)
            pe.wait_ge(check_ready, 1)
            nc.tensor.matmul(PS[0:1, BR1, 0:2], ones[:, :], check[:, :], start=True, stop=True).then_inc(check_summed, 1)
            pe.wait_ge(flags_ready, 1)
            redo = pe.value_load(flags[0:1, 0:1], min_val=0, max_val=1)
            wide = pe.value_load(flags[0:1, 1:2], min_val=0, max_val=1)
            with pe.If(redo != 0):
                with pe.Fori(0, NT) as t:
                    pe.wait_ge(g_cols, t * 2 + 1)
                    pe.wait_ge(cols_ready, 2 * NT + 1)
                    pe.wait_ge(g_ready, t * EPP + 1)
                    for c, (o_, w_) in enumerate(ACH):
                        nc.tensor.matmul(PS[:, c, 0:w_], zeros[:EP, :], iota_f16[:EP, 0:w_], start=True, stop=False)
                    with pe.Fori(0, RPP) as r:
                        for q in range(ROW):
                            pe.wait_ge(g_ready, t * EPP + r * ROW + (q + 1))
                            for c, (o_, w_) in enumerate(ACH):
                                ins = nc.tensor.matmul(PS[:, c, 0:w_], any_dst[:EP, q % 2, :],
                                                       onehot_src[:EP, q % 2, o_:o_ + w_], start=False, stop=False)
                            ins.then_inc(g_free, 1)
                    for c, (o_, w_) in enumerate(ACH):
                        ins = nc.tensor.matmul(PS[:, c, 0:w_], zeros[:EP, :], iota_f16[:EP, 0:w_], start=False, stop=True)
                    ins.then_inc(g_counts, 1)
                    turn_counts(g_saved, t + 1, g_turned)
                pe.wait_ge(g_cols, 2 * NT + 1)
                pe.wait_ge(g_written, 32 * NT)

            def feature_tile(j, parity, dt):
                banks = CHBANK[parity]
                pe.wait_ge(h1_freed, j * 3 + 1)
                pe.wait_ge(wst_lo, j + 1)
                for k in range(KF):
                    for m, (a, b) in enumerate(PRODUCTS):
                        for c, (o_, w_) in enumerate(CH):
                            ins = nc.tensor.matmul(PS[:, banks[c], 0:w_], W_st[:, a, k, :], HT[:, b, k, o_:o_ + w_],
                                                   start=k == 0 and m == 0, stop=False)
                ins.then_inc(wst_used, 1)
                pe.wait_ge(yst_lo, j * 2 + 2)
                pe.wait_ge(at_written, 32 * NT)
                for s in range(NT):
                    r = rows_of(s)
                    for part in (HI, LO):
                        for c, (o_, w_) in enumerate(CH):
                            ins = nc.tensor.matmul(PS[:, banks[c], 0:w_], y_st[:r, part, s, :].bitcast(dt),
                                                   AT[:r, s, o_:o_ + w_].bitcast(dt),
                                                   start=False, stop=s == NT - 1 and part == LO)
                ins.then_inc(h1_done, 1)

            def layer_two(half, dt):
                for t in range(NT):
                    pe.wait_ge(tile_freed, half * (2 * NT) + (t + 1))
                    if t in (0, 3, 6):
                        pe.wait_ge(h1_lo, KF + t // 3)
                    for k in range(KF):
                        if t == 0:
                            pe.wait_ge(w_lo, half * (2 * KF) + (2 * KF + k + 1))
                        ins = slab_products(RING34[t % 4], t, k, k == 0, k == KF - 1)
                        if k == KF - 1:
                            ins.then_inc(tile_done, 1)
                        elif t == NT - 1:
                            ins.then_inc(w_used, 1)
                for t in range(NT):
                    bank = RING34[(NT + t) % 4]
                    pe.wait_ge(tile_freed, half * (2 * NT) + (NT + t + 1))
                    for k in range(KF):
                        if t == 0:
                            pe.wait_ge(w_lo, half * (2 * KF) + (3 * KF + k + 1))
                        ins = slab_products(bank, t, k, k == 0, False)
                        if t == NT - 1:
                            ins.then_inc(w_used, 1)
                    if t == 0:
                        pe.wait_ge(tile_freed, half * (2 * NT) + (4 + NT))
                    for s in range(NT):
                        r = rows_of(s)
                        for part in (HI, LO):
                            ins = nc.tensor.matmul(PS[:rows_of(t), bank, :], AT[:r, s, t * P:t * P + rows_of(t)].bitcast(dt),
                                                   y2[:r, s, part, :].bitcast(dt),
                                                   start=False, stop=s == NT - 1 and part == LO)
                    ins.then_inc(tile_done, 1)

            for want, dt in ((0, F32R), (1, F32)):
                with pe.If(wide == want):
                    with pe.Fori(0, KF // 2) as q:
                        for parity in range(2):
                            feature_tile(q * 2 + parity, parity, dt)
                    with pe.Fori(0, 2) as half:
                        layer_two(half, dt)


def kernel(x, src, dst, L0_gnn_Ws1, L0_gnn_Wn1, L0_gnn_b1, L0_gnn_Ws2, L0_gnn_Wn2, L0_gnn_b2):
    import numpy as np
    import concourse.bacc as bacc
    from concourse.bass_utils import run_bass_kernel_spmd

    nc = bacc.Bacc("TRN2", target_bir_lowering=False, num_devices=1)
    arrays, args = {}, []
    for name, a in (("x", x), ("src", src), ("dst", dst), ("ws1", L0_gnn_Ws1), ("wn1", L0_gnn_Wn1), ("b1", L0_gnn_b1),
                    ("ws2", L0_gnn_Ws2), ("wn2", L0_gnn_Wn2), ("b2", L0_gnn_b2)):
        a = np.ascontiguousarray(a)
        arrays[name + "_in"] = a
        args.append(nc.dram_tensor(name + "_in", a.shape, mybir.dt.from_np(a.dtype), kind="ExternalInput").ap())
    args.append(nc.dram_tensor("out_0", (N, D), F32, kind="ExternalOutput").ap())
    gnn_kernel(nc, *args)
    r = run_bass_kernel_spmd(nc, [arrays], core_ids=[0])
    return r.results[0]["out_0"]
```

```python
import concourse.bass as bass
from concourse import mybir
from contextlib import ExitStack

F32 = mybir.dt.float32
F32R = mybir.dt.float32r
F16 = mybir.dt.float16
I32 = mybir.dt.int32
ALU = mybir.AluOpType
ACT = mybir.ActivationFunctionType

P = 128
N = 1250
D = 1024
E = 41250
KF = D // P
NT = -(-N // P)
LAST = N - (NT - 1) * P
NPAD = NT * P
HALF = D // 2
HI, LO = 0, 1
PRODUCTS = ((HI, HI), (HI, LO), (LO, HI))
CH = ((0, 418), (418, 416), (834, 416))
WIN = 32
NW = NPAD // WIN
WPT = P // WIN
ROW = 10
EROWS = E // ROW
SAMPLE = 3
EP = 125
EPP = E // EP
RPP = EPP // ROW
NSAMP = RPP // SAMPLE
SLOTS = 8
ACT_STEPS = (1, 5, 9)
SLAB_LAG = 6
EPS = 1e-5
EXACT = 4096
EARLY = 5


def up(size):
    return -(-size // 32) * 32


def rows_of(t):
    return LAST if t == NT - 1 else P


def stage1_order():
    order = []
    for g in range(NT // 2):
        tiles = [i for i in range(EARLY + 3 * g, EARLY + 3 * g + 3) if i < 2 * NT - 1]
        units = [("y1", i, k) for i in tiles for k in range(KF)]
        for n in (2 * g, 2 * g + 1):
            mine = units[len(units) * (n % 2) // 2:len(units) * (n % 2 + 1) // 2]
            for c in range(ROW + 1):
                order += mine[len(mine) * c // (ROW + 1):len(mine) * (c + 1) // (ROW + 1)]
                if c < ROW:
                    order.append(("count", n, c))
            if n < NT - 1:
                order.append(("turn", n))
    last = [("y1", 2 * NT - 1, k) for k in (5, 6, 7, 0, 1, 2, 3, 4)]
    return order + last[:3] + [("turn", NT - 1)] + last[3:6] + [("check",)] + last[6:]


def stage1_ends(*kinds):
    events = stage1_order()
    for p, event in enumerate(events):
        y1_ends = event[0] == "y1" and event[1] not in [e[1] for e in events[p + 1:] if e[0] == "y1"]
        if event[0] in kinds and (y1_ends or event[0] == "turn" or event[0] == "count" and event[2] == ROW - 1):
            yield p, event[:2]


def sync_order():
    ends = dict(stage1_ends("y1", "turn"))
    for p, event in enumerate(stage1_order()):
        if event[:2] == ("y1", NT - 1):
            yield ("slab", event[2])
        if event == ("turn", NT - 1):
            yield ("w_st", 0)
        if p in ends:
            yield ends[p]


def scalar_order():
    ends = dict(stage1_ends("y1", "count", "turn"))
    slabs = [p for p, event in enumerate(stage1_order()) if event[:2] == ("y1", NT - 1)]
    for p, event in enumerate(stage1_order()):
        if p in ends:
            yield ends[p]
        if event[0] == "count" and event[2] % 2:
            n, i = divmod(event[1] * ROW + event[2] + 2, ROW)
            if n < NT and i in ACT_STEPS:
                yield ("onehot", n, i)
        if p - SLAB_LAG in slabs:
            yield ("slab", slabs.index(p - SLAB_LAG))


def gnn_kernel(nc, x, src, dst, ws1, wn1, b1, ws2, wn2, b2, out):
    edge_rows = nc.dram_tensor("edge_rows", (EROWS + P + 3, 2 * ROW), F32, kind="Internal").ap()
    y1_dram = nc.dram_tensor("y1_dram", (N, D), F32, kind="Internal").ap()

    ctx = ExitStack()
    with ctx:
        base = up(nc.sbuf_base)

        def at(name, shape, dt, offset):
            return nc.alloc_sbuf_tensor_at(name, shape, dt, offset=base + offset)

        def sem(name):
            return ctx.enter_context(nc.semaphore(name))

        AT0 = 2 * KF * N * 4
        R0 = AT0 + NT * NPAD * 4
        W0 = R0 + 2 * HALF * 4 * NT
        HT = at("HT", [P, 2, KF, N], F32R, 0)
        AT = at("AT", [P, NT, NPAD], F32R, AT0)
        xin = at("xin", [P, NT, D], F32, AT0)
        hbuf = at("hbuf", [P, 2, D], F32, AT0 + NT * D * 4)
        W = at("W", [P, KF, 2, HALF], F32R, W0)
        W_raw = at("W_raw", [P, KF, 2, HALF], F32, W0)
        o = R0
        onehot_src = at("onehot_src", [P, SLOTS, N], F16, o); o += up(SLOTS * N * 2)
        iota_f16 = at("iota_f16", [P, N], F16, o); o += up(N * 2)
        DST0 = o
        onehot_dst = at("onehot_dst", [P, WPT * ROW, WIN], F16, o); o += up(WPT * ROW * WIN * 2)
        window_edges = at("window_edges", [P, NW, 2 * ROW], F32, o); o += up(NW * 2 * ROW * 4)
        A_rows = at("A_rows", [P, N], F32, o); o += up(N * 4)
        A_cols = at("A_cols", [P, NT, P], F32, o); o += up(NT * P * 4)
        ident = at("ident", [P, P], F32, o); o += up(P * 4)
        assert o <= W0, o - W0
        o = W0 + KF * 2 * HALF * 4
        y1_out = at("y1_out", [P, 2, HALF], F32, o); o += up(2 * HALF * 4)
        onehot_dst_odd = at("onehot_dst_odd", [P, WPT * ROW, WIN], F16, o)
        edges = at("edges", [EP, RPP, 2, ROW], F32, o); o += up(EPP * 2 * 4)
        ONEHOT_DST = (onehot_dst, onehot_dst_odd)
        C0 = o
        edge_ints = at("edge_ints", [EP, 2, EPP], I32, R0)
        pad_row = at("pad_row", [P, 2 * ROW], F32, R0 + up(2 * EPP * 4))
        h1T = at("h1T", [P, KF, N], F32, R0)
        ST0 = W0 + 5 * 2 * HALF * 4
        W_st = at("W_st", [P, 2, KF, P], F32R, ST0)
        W_st_raw = at("W_st_raw", [P, 2, KF, P], F32, ST0)
        y_st = at("y_st", [P, 2, NT, P], F32R, ST0 + 2 * D * 4)
        y_st_raw = at("y_st_raw", [P, 2, NT, P], F32, ST0 + 2 * D * 4)
        y2 = at("y2", [P, NT, 2, HALF], F32R, R0)
        x_out = at("x_out", [P, 2, HALF], F32, W0 + KF * 2 * HALF * 4)
        b2_sb = at("b2_sb", [P, HALF], F32, W0 + KF * 2 * HALF * 4 + 2 * HALF * 4)
        o = max(C0, ST0 + 2 * D * 4 + 2 * NPAD * 4)
        b1_sb = at("b1_sb", [P, KF], F32, o); o += up(KF * 4)
        stats = at("stats", [P, 2, 2, 6], F32, o); o += up(2 * 2 * 6 * 4)
        mv = at("mv", [P, 2, 2], F32, o); o += 32
        iota32 = at("iota32", [P, WIN], F32, o); o += up(WIN * 4)
        degree = at("degree", [P, NT], F32, o); o += 64
        check = at("check", [P, 2], F32, o); o += 32
        ones = at("ones", [P, 1], F32, o); o += 32
        norm = at("norm", [P, 2, 2], F32, o); o += 32
        unused = at("unused", [P, 8], F32, o); o += 32
        minus_half = at("minus_half", [P, 1], F32, o); o += 32
        flags_f = at("flags_f", [P, 4], F32, o); o += 32
        flags = at("flags", [1, 2], I32, o); o += 32
        early = AT0 + (NT + 2) * D * 4
        samples = at("samples", [EP, NW], F32, early)
        row_f = at("row_f", [1, NW], F32, early + NW * 4)
        row_i = at("row_i", [1, NW], I32, early + 2 * NW * 4)
        win_start = at("win_start", [P, NW], F32, early + 3 * NW * 4)
        any_dst = at("any_dst", [P, 2, P], F16, DST0)
        zeros = at("zeros", [P, P], F16, DST0 + 2 * P * 2)
        assert base + o <= nc.sbuf_usable_end, (base + o, nc.sbuf_usable_end)

        PS = ctx.enter_context(nc.psum_tensor("PS", [P, 8, 512], F32))
        PSF = PS[:, :, :].rearrange("p b n -> p (b n)")

        edges_in = sem("edges_in"); consts_in = sem("consts_in"); b2_in = sem("b2_in")
        x_in_t = [sem(f"x_in_{t}") for t in range(NT)]
        setup = sem("setup"); pool_self = sem("pool_self"); dve_self = sem("dve_self"); act_self = sem("act_self")
        edges_cast = sem("edges_cast"); rows_saved = sem("rows_saved"); edges_back = sem("edges_back")
        sampled = sem("sampled"); counted = sem("counted"); row_found = sem("row_found")
        windows_in = [sem(f"windows_in_{a}") for a in range(NT)]
        rebased = sem("rebased")
        var_ready = sem("var_ready"); norm_self = sem("norm_self"); norm_ready = sem("norm_ready")
        h_ready = sem("h_ready"); h_turned = sem("h_turned"); ht_hi = sem("ht_hi"); ht_lo = sem("ht_lo")
        w_raw = [sem(f"w_raw_{k}") for k in range(KF)]
        w_hi = sem("w_hi"); w_lo = sem("w_lo"); w_used = sem("w_used")
        dst_ready = sem("dst_ready"); src_ready = sem("src_ready"); act_src_ready = sem("act_src_ready")
        src_free = sem("src_free"); counts_saved = sem("counts_saved")
        turned = sem("turned"); cols_ready = sem("cols_ready"); at_written = sem("at_written")
        y1_done = sem("y1_done"); y1_freed = sem("y1_freed"); y1_saved = [sem(f"y1_saved_{i}") for i in range(2)]
        check_ready = sem("check_ready"); check_summed = sem("check_summed"); flags_ready = sem("flags_ready")
        g_ready = sem("g_ready"); g_free = sem("g_free"); g_counts = sem("g_counts"); g_saved = sem("g_saved")
        g_turned = sem("g_turned"); g_cols = sem("g_cols"); g_written = sem("g_written"); g_self = sem("g_self")
        wst_in = sem("wst_in"); wst_hi = sem("wst_hi"); wst_lo = sem("wst_lo"); wst_used = sem("wst_used")
        yst_in = sem("yst_in"); yst_hi = sem("yst_hi"); yst_lo = sem("yst_lo")
        h1_done = sem("h1_done"); h1_freed = sem("h1_freed"); h1_hi = sem("h1_hi"); h1_lo = sem("h1_lo")
        tile_done = sem("tile_done"); y2_hi = sem("y2_hi"); tile_freed = sem("tile_freed")
        x2_in = [sem(f"x2_in_{i}") for i in range(2)]; x2_biased = sem("x2_biased")
        out_saved = [sem(f"out_saved_{i}") for i in range(2)]

        RING34 = (6, 7, 0, 1)
        BR1, Y1_BANKS = 6, 2
        TURN = 3 * 512
        ACH = ((0, 512), (512, 512), (1024, N - 1024))
        CHBANK = ((0, 1, 2), (3, 4, 5))

        block = ctx.enter_context(nc.Block())

        @block.sync
        def _(sp):
            def slab_used(use, k):
                if k == KF - 1 and use == 0:
                    sp.wait_ge(y1_done, NT)
                elif k == KF - 1 and use % 2 == 0:
                    sp.wait_ge(tile_done, use // 2 * 2 * NT - NT)
                else:
                    sp.wait_ge(w_used, sum((KF - 1, KF - 1, KF - 1, KF, KF - 1, KF)[:use]) + k + 1)

            def load_w(m, half, k):
                sp.dma_start(W_raw[:, k, LO, :],
                             m[k * P:(k + 1) * P, half * HALF:(half + 1) * HALF]).then_inc(w_raw[k], 16)

            def load_x_tile(t):
                r = rows_of(t)
                sp.dma_start(xin[:r, t, :], x[t * P:t * P + r, :]).then_inc(x_in_t[t], 16)

            load_x_tile(0)
            sp.dma_start(edge_ints[:, 0, :], src.rearrange("(p e) -> p e", p=EP)).then_inc(edges_in, 16)
            sp.dma_start(edge_ints[:, 1, :], dst.rearrange("(p e) -> p e", p=EP)).then_inc(edges_in, 16)
            for t in range(1, 5):
                load_x_tile(t)
                if t < 4:
                    load_w(wn1, 0, 2 * (t - 1))
                    load_w(wn1, 0, 2 * (t - 1) + 1)
            sp.wait_ge(setup, 1)
            sp.dma_start(edge_rows[EROWS:EROWS + P, :], pad_row[:, :]).then_inc(rows_saved, 16)
            sp.wait_ge(edges_cast, 2)
            sp.dma_start(edge_rows[0:EROWS, :].rearrange("(p r) c -> p (r c)", p=EP),
                         edges[:, :, :, :].rearrange("p r a c -> p (r a c)")).then_inc(rows_saved, 16)

            load_w(wn1, 0, 6)
            load_w(wn1, 0, 7)
            for t in range(5, NT):
                load_x_tile(t)
            with nc.allow_non_contiguous_dma("4 KB bias as a column for each feature tile"):
                sp.dma_start(b1_sb[:, :], b1.rearrange("(k p) -> p k", p=P)).then_inc(consts_in, 16)

            sp.wait_ge(rows_saved, 32)
            sp.wait_ge(row_found, 1)

            def load_windows(a):
                with sp.Fori(a * WPT, (a + 1) * WPT) as w:
                    r = sp.value_load(row_i[0:1, bass.ds(w, 1)], min_val=0, max_val=EROWS)
                    sp.dma_start(window_edges[:, bass.ds(w, 1), :],
                                 edge_rows[bass.ds(r, P), :].unsqueeze(1)).then_inc(windows_in[a], 16)

            for a in range(2):
                load_windows(a)

            def save_y1(i):
                (half, t), r = divmod(i, NT), rows_of(i % NT)
                sp.wait_ge(y1_freed, Y1_BANKS + i + 1)
                sp.dma_start(y1_dram[t * P:t * P + r, half * HALF:(half + 1) * HALF],
                             y1_out[:r, i % 2, :]).then_inc(y1_saved[i % 2], 16)

            for i in range(EARLY):
                save_y1(i)
                load_windows(2 + i)

            def load_w_st(j):
                sp.dma_start(W_st_raw[:, LO, :, :],
                             ws1[:, j * P:(j + 1) * P].rearrange("(k p) c -> p k c", p=P)).then_inc(wst_in, 16)

            for what, n in sync_order():
                if what == "slab":
                    slab_used(0, n)
                    load_w(wn1, 1, n)
                elif what == "w_st":
                    sp.wait_ge(w_used, KF - 1 + 3)
                    load_w_st(0)
                elif what == "turn":
                    sp.wait_ge(cols_ready, 2 * (n + 1) + 1)
                    sp.dma_start(AT[:, 0:NT - 1, n * P:(n + 1) * P].bitcast(F32), A_cols[:, 0:NT - 1, :]).then_inc(at_written, 16)
                    sp.dma_start(AT[:LAST, NT - 1, n * P:(n + 1) * P].bitcast(F32), A_cols[:LAST, NT - 1, :]).then_inc(at_written, 16)
                else:
                    save_y1(n)
                    if n + 2 < NT:
                        load_windows(n + 2)

            sp.wait_ge(flags_ready, 1)
            redo = sp.value_load(flags[0:1, 0:1], min_val=0, max_val=1)
            with sp.If(redo != 0):
                sp.dma_start(edges[:, :, :, :].rearrange("p r a c -> p (r a c)"),
                             edge_rows[0:EROWS, :].rearrange("(p r) c -> p (r c)", p=EP)).then_inc(edges_back, 16)
                sp.wait_ge(at_written, NT * 32)
                for t in range(NT):
                    sp.wait_ge(g_cols, 2 * t + 3)
                    sp.dma_start(AT[:, 0:NT - 1, t * P:(t + 1) * P].bitcast(F32), A_cols[:, 0:NT - 1, :]).then_inc(g_written, 16)
                    sp.dma_start(AT[:LAST, NT - 1, t * P:(t + 1) * P].bitcast(F32), A_cols[:LAST, NT - 1, :]).then_inc(g_written, 16)
                    sp.wait_ge(g_written, 32 * t + 32)
                sp.wait_ge(g_self, NT)

            for j in range(KF):
                if j:
                    sp.wait_ge(wst_used, j)
                    load_w_st(j)
                sp.wait_ge(y1_saved[0], NT * 16)
                sp.wait_ge(y1_saved[1], NT * 16)
                if j:
                    sp.wait_ge(h1_done, j)
                sp.dma_start(y_st_raw[:, LO, 0:NT - 1, :],
                             y1_dram[0:(NT - 1) * P, j * P:(j + 1) * P].rearrange("(s p) c -> p s c", p=P)).then_inc(yst_in, 16)
                sp.dma_start(y_st_raw[:LAST, LO, NT - 1, :],
                             y1_dram[(NT - 1) * P:N, j * P:(j + 1) * P]).then_inc(yst_in, 16)

            sp.wait_ge(h1_done, KF - 1)
            for k in range(KF):
                if k == 5:
                    sp.wait_ge(wst_used, KF)
                if k == 7:
                    sp.wait_ge(h1_done, KF)
                load_w(wn2, 0, k)

            def load_x(t, half, r, n):
                if n >= 2:
                    sp.wait_ge(out_saved[n % 2], 16 * (n // 2))
                sp.dma_start(x_out[:r, n % 2, :],
                             x[t * P:t * P + r, half * HALF:(half + 1) * HALF]).then_inc(x2_in[n % 2], 16)

            for half in range(2):
                if half:
                    sp.wait_ge(x2_biased, NT)
                else:
                    sp.wait_ge(h1_done, KF)
                sp.dma_start(b2_sb[:, :], b2[half * HALF:(half + 1) * HALF].partition_broadcast(P)).then_inc(b2_in, 16)
                for k in range(KF):
                    slab_used(2 + 2 * half, k)
                    load_w(ws2, half, k)
                for t in range(NT):
                    n = half * NT + t
                    load_x(t, half, rows_of(t), n)
                    if t == NT - 1 and half == 0:
                        for k in range(KF):
                            slab_used(3, k)
                            load_w(wn2, 1, k)
                    if t:
                        r = rows_of(t - 1)
                        sp.wait_ge(tile_freed, 4 + 2 * NT * half + NT + t)
                        sp.dma_start(out[(t - 1) * P:(t - 1) * P + r, half * HALF:(half + 1) * HALF],
                                     x_out[:r, (n - 1) % 2, :]).then_inc(out_saved[(n - 1) % 2], 16)
                sp.wait_ge(tile_freed, 4 + 2 * NT * (half + 1))
                sp.dma_start(out[(NT - 1) * P:N, half * HALF:(half + 1) * HALF],
                             x_out[:LAST, (NT - 1) % 2, :]).then_inc(out_saved[(NT - 1) % 2], 16)
            for i in range(2):
                sp.wait_ge(out_saved[i], NT * 16)

        @block.gpsimd
        def _(pool):
            nc.gpsimd.memset(minus_half[:, :], -0.5).then_inc(pool_self, 1)
            nc.gpsimd.memset(pad_row[:, :], -1.0).then_inc(setup, 1)
            nc.gpsimd.iota(win_start[:, :], pattern=[[WIN, NW]], base=0, channel_multiplier=0,
                           allow_small_or_imprecise_dtypes=True).then_inc(setup, 1)
            nc.gpsimd.memset(unused[:, 0:1], 0.0).then_inc(cols_ready, 1)
            nc.gpsimd.memset(unused[:, 1:2], 0.0).then_inc(g_cols, 1)
            nc.gpsimd.memset(unused[:, 2:3], 0.0).then_inc(y1_freed, Y1_BANKS)
            nc.gpsimd.memset(unused[:, 3:4], 0.0).then_inc(h1_freed, 3 + 1)
            nc.gpsimd.memset(unused[:, 4:5], 0.0).then_inc(tile_freed, 4)
            nc.gpsimd.memset(ident[:, :], 0.0).then_inc(pool_self, 1)
            pool.wait_ge(pool_self, 2)
            nc.gpsimd.affine_select(out=ident[:, :], in_=ident[:, :], compare_op=ALU.not_equal, fill=1.0,
                                    base=0, pattern=[[-1, P]], channel_multiplier=1).then_inc(setup, 1)
            nc.gpsimd.memset(ones[:, :], 1.0).then_inc(setup, 1)

            def w_low(n, k):
                pool.wait_ge(w_hi, n + 1)
                nc.gpsimd.tensor_tensor(W[:, k, LO, :], W_raw[:, k, LO, :], W[:, k, HI, :].bitcast(F32),
                                        ALU.subtract).then_inc(w_lo, 1)

            def w_low_pair(t):
                if 0 <= 2 * t < KF:
                    w_low(2 * t, 2 * t)
                    w_low(2 * t + 1, 2 * t + 1)

            for t in range(NT):
                r, m = rows_of(t), mv[:rows_of(t), t % 2, :]
                pool.wait_ge(var_ready, t + 1)
                nc.gpsimd.tensor_scalar(m[:, 1:2], m[:, 1:2], EPS, None, ALU.add)
                nc.gpsimd.tensor_scalar(m[:, 0:1], m[:, 0:1], -1.0, None, ALU.mult).then_inc(norm_self, 1)
                pool.wait_ge(norm_self, 2 * t + 1)
                if t >= 2:
                    pool.wait_ge(h_ready, t - 1)
                nc.gpsimd.tensor_tensor(norm[:r, t % 2, 1:2], m[:, 1:2], minus_half[:r, :], ALU.pow).then_inc(norm_self, 1)
                pool.wait_ge(norm_self, 2 * t + 2)
                nc.gpsimd.tensor_tensor(norm[:r, t % 2, 0:1], m[:, 0:1], norm[:r, t % 2, 1:2], ALU.mult).then_inc(norm_ready, 1)
                w_low_pair(t - 1)
                if t == 1:
                    nc.gpsimd.iota(iota32[:, :], pattern=[[1, WIN]], base=0, channel_multiplier=0,
                                   allow_small_or_imprecise_dtypes=True).then_inc(pool_self, 1)
                    nc.gpsimd.iota(iota_f16[:, :], pattern=[[1, N]], base=0, channel_multiplier=0,
                                   allow_small_or_imprecise_dtypes=True).then_inc(src_free, SLOTS)

            for a in range(NT):
                pool.wait_ge(windows_in[a], WPT * 16)
                tile_edges = window_edges[:, a * WPT:(a + 1) * WPT, ROW:]
                nc.gpsimd.tensor_tensor(tile_edges, tile_edges,
                                        win_start[:, a * WPT:(a + 1) * WPT].unsqueeze(2).to_broadcast([P, WPT, ROW]),
                                        ALU.subtract).then_inc(rebased, 1)
            for k in range(KF):
                w_low(KF + k, k)

            for half in range(2):
                pool.wait_ge(b2_in, 16 * (half + 1))
                for t in range(NT):
                    i, r = half * NT + t, rows_of(t)
                    pool.wait_ge(x2_in[i % 2], 16 * (i // 2 + 1))
                    nc.gpsimd.tensor_tensor(x_out[:r, i % 2, :], x_out[:r, i % 2, :], b2_sb[:r, :],
                                            ALU.add).then_inc(x2_biased, 1)

        @block.scalar
        def _(act):
            def w_high(n, k):
                act.wait_ge(w_raw[k], 16 * (n // KF + 1))
                nc.scalar.activation(W[:, k, HI, :], W_raw[:, k, LO, :], ACT.Copy).then_inc(w_hi, 1)

            def save_y1(i):
                r = rows_of(i % NT)
                act.wait_ge(y1_done, i + 1)
                if i >= 2:
                    act.wait_ge(y1_saved[i % 2], 16 * (i // 2))
                nc.scalar.activation(y1_out[:r, i % 2, :], PS[:r, BR1 + i % Y1_BANKS, :], ACT.Copy).then_inc(y1_freed, 1)

            def transposed_high(t):
                r, b = rows_of(t), 2 * (t % 2)
                act.wait_ge(h_turned, t + 1)
                nc.scalar.activation(HT[:, HI, :, t * P:t * P + r],
                                     PSF[:, b * 512:b * 512 + D].rearrange("p (k c) -> p k c", k=KF)[:, :, 0:r],
                                     ACT.Copy).then_inc(ht_hi, 1)

            for t in range(NT):
                r = rows_of(t)
                act.wait_ge(x_in_t[t], 16)
                act.wait_ge(norm_ready, t + 1)
                if t >= 2:
                    act.wait_ge(h_turned, t - 1)
                nc.scalar.activation(hbuf[:r, t % 2, :], xin[:r, t, :], ACT.Relu, bias=norm[:r, t % 2, 0:1],
                                     scale=norm[:r, t % 2, 1:2]).then_inc(h_ready, 1)
                if 2 * t < KF:
                    w_high(2 * t, 2 * t)
                    w_high(2 * t + 1, 2 * t + 1)
                if t:
                    transposed_high(t - 1)
                if t in (6, 8):
                    save_y1((t - 6) // 2)
            transposed_high(NT - 1)
            for i in range(2, EARLY):
                save_y1(i)

            def w_st_high(j):
                act.wait_ge(wst_in, 16 * j + 16)
                nc.scalar.activation(W_st[:, HI, :, :], W_st_raw[:, LO, :, :], ACT.Copy).then_inc(wst_hi, 1)

            def onehot(n, i):
                slot = onehot_src[:, SLOTS - 1, :]
                act.wait_ge(rebased, n + 1)
                act.wait_ge(src_free, n * WPT * ROW + (i + 1) * WPT)
                nc.scalar.activation(slot, iota_f16[:, :], ACT.Abs, scale=-1.0,
                                     bias=window_edges[:, (n + 1) * WPT - 1, i:i + 1]).then_inc(act_self, 1)
                act.wait_ge(act_self, n * len(ACT_STEPS) + ACT_STEPS.index(i) + 1)
                nc.scalar.activation(slot, slot, ACT.Relu, scale=-1.0, bias=1.0).then_inc(act_src_ready, 1)

            onehot(0, 1)
            for what, n, *step in scalar_order():
                if what == "slab":
                    w_high(KF + n, n)
                elif what == "onehot":
                    onehot(n, step[0])
                elif what == "count":
                    act.wait_ge(src_free, SLOTS + (n + 1) * WPT * ROW)
                    if n:
                        act.wait_ge(turned, n)
                    nc.scalar.activation(A_rows[:, :], PSF[:, 0:N], ACT.Copy,
                                         accum_out=degree[:, n:n + 1]).then_inc(counts_saved, 1)
                elif what == "turn":
                    act.wait_ge(turned, n + 1)
                    if n:
                        act.wait_ge(at_written, 32 * n)
                    nc.scalar.activation(A_cols[:, 0:NT - 1, :],
                                         PSF[:, TURN:TURN + (NT - 1) * P].rearrange("p (s c) -> p s c", s=NT - 1), ACT.Copy).then_inc(cols_ready, 1)
                    nc.scalar.activation(A_cols[:LAST, NT - 1, :], PSF[:LAST, TURN + (NT - 1) * P:TURN + NT * P], ACT.Copy).then_inc(cols_ready, 1)
                else:
                    if n == 2 * NT - 1:
                        w_st_high(0)
                    save_y1(n)

            act.wait_ge(flags_ready, 1)
            redo = act.value_load(flags[0:1, 0:1], min_val=0, max_val=1)
            with act.If(redo != 0):
                act.wait_ge(at_written, 32 * NT)
                for t in range(NT):
                    act.wait_ge(g_counts, t + 1)
                    nc.scalar.activation(A_rows[:, :], PSF[:, 0:N], ACT.Copy).then_inc(g_saved, 1)
                    act.wait_ge(g_turned, t + 1)
                    if t:
                        act.wait_ge(g_written, 32 * t)
                    nc.scalar.activation(A_cols[:, 0:NT - 1, :],
                                         PSF[:, TURN:TURN + (NT - 1) * P].rearrange("p (s c) -> p s c", s=NT - 1), ACT.Copy).then_inc(g_cols, 1)
                    nc.scalar.activation(A_cols[:LAST, NT - 1, :], PSF[:LAST, TURN + (NT - 1) * P:TURN + NT * P], ACT.Copy).then_inc(g_cols, 1)
                act.wait_ge(g_written, 32 * NT)

            def stationary_high(j):
                w_st_high(j)
                y_st_high(j)

            def y_st_high(j):
                act.wait_ge(yst_in, 32 * j + 32)
                nc.scalar.activation(y_st[:, HI, 0:NT - 1, :], y_st_raw[:, LO, 0:NT - 1, :], ACT.Copy).then_inc(yst_hi, 1)
                nc.scalar.activation(y_st[:LAST, HI, NT - 1, :], y_st_raw[:LAST, LO, NT - 1, :], ACT.Copy).then_inc(yst_hi, 1)

            def h1_save(j, parity):
                act.wait_ge(h1_done, j + 1)
                for c, (o_, w_) in enumerate(CH):
                    nc.scalar.activation(h1T[:, bass.ds(j, 1), o_:o_ + w_], PS[:, CHBANK[parity][c], 0:w_].unsqueeze(1),
                                         ACT.Identity, bias=b1_sb[:, bass.ds(j, 1)]).then_inc(h1_freed, 1)

            act.wait_ge(consts_in, 16)
            y_st_high(0)
            act.wait_ge(at_written, 32 * NT)
            with act.Fori(0, KF // 2 - 1) as q:
                for parity in range(2):
                    stationary_high(2 * q + parity + 1)
                    h1_save(2 * q + parity, parity)
            stationary_high(KF - 1)
            h1_save(KF - 2, 0)
            for k in range(5):
                w_high(2 * KF + k, k)
            act.wait_ge(wst_used, KF)
            act.wait_ge(h1_freed, 1 + 3 * KF)
            for k in range(KF - 1):
                nc.scalar.activation(HT[:, HI, k, :], h1T[:, k, :], ACT.Copy).then_inc(h1_hi, 1)
            for k in (5, 6):
                w_high(2 * KF + k, k)
            act.wait_ge(h1_done, KF)
            for c, (o_, w_) in enumerate(CH):
                nc.scalar.activation(HT[:, HI, KF - 1, o_:o_ + w_], PS[:, CHBANK[1][c], 0:w_],
                                     ACT.Identity, bias=b1_sb[:, KF - 1:KF]).then_inc(h1_hi, 1)
            w_high(3 * KF - 1, KF - 1)

            n = 3 * KF
            for half in range(2):
                for t in range(NT):
                    if t == NT - 1:
                        for k in range(KF):
                            w_high(n, k)
                            n += 1
                    r, i = rows_of(t), 2 * NT * half + t
                    act.wait_ge(tile_done, i + 1)
                    nc.scalar.activation(y2[:r, t, HI, :], PS[:r, RING34[i % 4], :], ACT.Copy).then_inc(y2_hi, 1)
                if half == 0:
                    for k in range(KF):
                        w_high(n, k)
                        n += 1

        @block.vector
        def _(dve):
            count = [0]

            def chain(ins):
                ins.then_inc(dve_self, 1)
                count[0] += 1
                dve.wait_ge(dve_self, count[0])

            def statistics(t):
                r = rows_of(t)
                dve.wait_ge(x_in_t[t], 16)
                if t >= 2:
                    dve.wait_ge(norm_ready, t - 1)
                nc.vector.bn_stats(stats[:r, t % 2, 0, :], xin[:r, t, 0:HALF])
                chain(nc.vector.bn_stats(stats[:r, t % 2, 1, :], xin[:r, t, HALF:D]))
                nc.vector.bn_aggr(mv[:r, t % 2, :], stats[:r, t % 2, :, :].rearrange("p a b -> p (a b)")).then_inc(var_ready, 1)

            def low_of_h(t):
                r, b = rows_of(t), 2 * (t % 2)
                dve.wait_ge(ht_hi, t + 1)
                nc.vector.tensor_tensor(
                    HT[:, LO, :, t * P:t * P + r],
                    PSF[:, b * 512:b * 512 + D].rearrange("p (k c) -> p k c", k=KF)[:, :, 0:r],
                    HT[:, HI, :, t * P:t * P + r].bitcast(F32), ALU.subtract).then_inc(ht_lo, 1)

            def sample_edges():
                dve.wait_ge(edges_in, 32)
                for a in range(2):
                    nc.vector.tensor_copy(edges[:, :, a, :], edge_ints[:, a, :].rearrange("p (r c) -> p r c", c=ROW)).then_inc(edges_cast, 1)
                dve.wait_ge(edges_cast, 2)
                dve.wait_ge(setup, 2)
                for q in range(NSAMP):
                    s = edges[:, SAMPLE * q, 1, 0:1]
                    if q == 0:
                        chain(nc.vector.tensor_scalar(samples[:, :], win_start[:EP, :], s, None, ALU.is_gt))
                    else:
                        ins = nc.vector.scalar_tensor_tensor(samples[:, :], win_start[:EP, :], s, samples[:, :], ALU.is_gt, ALU.add)
                        if q < NSAMP - 1:
                            chain(ins)
                        else:
                            ins.then_inc(sampled, 1)

            for t in range(NT):
                statistics(t)
                if t >= 2:
                    low_of_h(t - 2)
                if t == 2:
                    sample_edges()
                if t == 3:
                    dve.wait_ge(counted, 1)
                    chain(nc.vector.tensor_scalar(row_f[:, :], PS[0:1, 5, 0:NW], float(SAMPLE), float(-SAMPLE), ALU.mult, ALU.add))
                    chain(nc.vector.tensor_scalar(row_f[:, :], row_f[:, :], 0.0, None, ALU.max))
                    nc.vector.tensor_copy(row_i[:, :], row_f[:, :]).then_inc(row_found, 1)
            low_of_h(NT - 2)
            low_of_h(NT - 1)

            dve.wait_ge(pool_self, 3)
            with dve.Fori(0, NT // 2) as pair:
                for odd in range(2):
                    a = pair * 2 + odd
                    dve.wait_ge(rebased, a + 1)
                    nc.vector.tensor_tensor(
                        ONEHOT_DST[odd][:, :, :].rearrange("p (w i) m -> p w i m", w=WPT),
                        window_edges[:, bass.ds(a * WPT, WPT), ROW:].unsqueeze(3).to_broadcast([P, WPT, ROW, WIN]),
                        iota32[:, :].unsqueeze(1).unsqueeze(1).to_broadcast([P, WPT, ROW, WIN]),
                        ALU.is_equal).then_inc(dst_ready, 1)
                    for i in range(ROW):
                        for j in range(WPT - (i in ACT_STEPS)):
                            q = i * WPT + j
                            dve.wait_ge(src_free, pair * (2 * WPT * ROW) + (odd * WPT * ROW + q + 1))
                            nc.vector.tensor_scalar(onehot_src[:, q % SLOTS, :], iota_f16[:, :],
                                                    window_edges[:, bass.ds(a * WPT + j, 1), i], None,
                                                    ALU.is_equal).then_inc(src_ready, 1)

            dve.wait_ge(counts_saved, NT)
            nc.vector.reduce_sum(check[:, 0:1], degree[:, :], axis=mybir.AxisListType.X)
            chain(nc.vector.reduce_max(check[:, 1:2], degree[:, :], axis=mybir.AxisListType.X))
            nc.vector.tensor_scalar(check[:, 1:2], check[:, 1:2], float(EXACT), None, ALU.is_gt).then_inc(check_ready, 1)
            dve.wait_ge(check_summed, 1)
            nc.vector.tensor_scalar(flags_f[0:1, 0:1], PS[0:1, 0, 0:1], float(E), None, ALU.not_equal)
            chain(nc.vector.tensor_scalar(flags_f[0:1, 1:2], PS[0:1, 0, 1:2], 0.0, None, ALU.is_gt))
            chain(nc.vector.tensor_tensor(flags_f[0:1, 1:2], flags_f[0:1, 0:1], flags_f[0:1, 1:2], ALU.max))
            nc.vector.tensor_copy(flags[0:1, :], flags_f[0:1, 0:2]).then_inc(flags_ready, 1)

            dve.wait_ge(flags_ready, 1)
            redo = dve.value_load(flags[0:1, 0:1], min_val=0, max_val=1)
            with dve.If(redo != 0):
                nc.vector.memset(zeros[:, :], 0.0).then_inc(g_free, 2)
                dve.wait_ge(edges_back, 16)
                with dve.Fori(0, NT) as t:
                    with dve.Fori(0, RPP) as r:
                        for q in range(ROW):
                            dve.wait_ge(g_free, t * EPP + r * ROW + (q + 1))
                            nc.vector.tensor_scalar(onehot_src[:EP, q % 2, :], iota_f16[:EP, :],
                                                    edges[:, bass.ds(r, 1), 0, q], None, ALU.is_equal)
                            nc.vector.tensor_scalar(any_dst[:EP, q % 2, :], iota_f16[:EP, 0:P],
                                                    edges[:, bass.ds(r, 1), 1, q], None, ALU.is_equal).then_inc(g_ready, 1)
                    dve.wait_ge(g_ready, t * EPP + EPP)
                    nc.vector.tensor_scalar(edges[:, :, 1, :], edges[:, :, 1, :], float(P), None, ALU.subtract).then_inc(g_self, 1)
                    dve.wait_ge(g_self, t + 1)

            def w_low(n, k):
                dve.wait_ge(w_hi, n + 1)
                nc.vector.tensor_tensor(W[:, k, LO, :], W_raw[:, k, LO, :], W[:, k, HI, :].bitcast(F32),
                                        ALU.subtract).then_inc(w_lo, 1)

            with dve.Fori(0, KF) as j:
                dve.wait_ge(wst_hi, j + 1)
                nc.vector.tensor_tensor(W_st[:, LO, :, :], W_st_raw[:, LO, :, :], W_st[:, HI, :, :].bitcast(F32),
                                        ALU.subtract).then_inc(wst_lo, 1)
                dve.wait_ge(yst_hi, 2 * j + 2)
                nc.vector.tensor_tensor(y_st[:, LO, 0:NT - 1, :], y_st_raw[:, LO, 0:NT - 1, :],
                                        y_st[:, HI, 0:NT - 1, :].bitcast(F32), ALU.subtract).then_inc(yst_lo, 1)
                nc.vector.tensor_tensor(y_st[:LAST, LO, NT - 1, :], y_st_raw[:LAST, LO, NT - 1, :],
                                        y_st[:LAST, HI, NT - 1, :].bitcast(F32), ALU.subtract).then_inc(yst_lo, 1)
            for k in range(5):
                w_low(2 * KF + k, k)
            for k in range(KF - 1):
                dve.wait_ge(h1_hi, k + 1)
                nc.vector.tensor_tensor(HT[:, LO, k, :], h1T[:, k, :], HT[:, HI, k, :].bitcast(F32),
                                        ALU.subtract).then_inc(h1_lo, 1)
            for k in (5, 6):
                w_low(2 * KF + k, k)
            for c, (o_, w_) in enumerate(CH):
                dve.wait_ge(h1_hi, KF + c)
                nc.vector.scalar_tensor_tensor(HT[:, LO, KF - 1, o_:o_ + w_], PS[:, CHBANK[1][c], 0:w_],
                                               b1_sb[:, KF - 1:KF], HT[:, HI, KF - 1, o_:o_ + w_].bitcast(F32),
                                               ALU.add, ALU.subtract).then_inc(h1_lo, 1)

            w_low(3 * KF - 1, KF - 1)

            for half in range(2):
                for t in range(NT):
                    r, n = rows_of(t), 2 * NT * half + t
                    if t == NT - 1:
                        for k in range(KF):
                            w_low((3 + 2 * half) * KF + k, k)
                    dve.wait_ge(y2_hi, NT * half + t + 1)
                    nc.vector.tensor_tensor(y2[:r, t, LO, :], PS[:r, RING34[n % 4], :], y2[:r, t, HI, :].bitcast(F32),
                                            ALU.subtract).then_inc(tile_freed, 1)
                for t in range(NT):
                    r, n = rows_of(t), 2 * NT * half + NT + t
                    if t == NT - 1 and half == 0:
                        for k in range(KF):
                            w_low(4 * KF + k, k)
                    dve.wait_ge(x2_biased, NT * half + t + 1)
                    dve.wait_ge(tile_done, n + 1)
                    i = (NT * half + t) % 2
                    nc.vector.tensor_tensor(x_out[:r, i, :], PS[:r, RING34[n % 4], :], x_out[:r, i, :],
                                            ALU.add).then_inc(tile_freed, 1)

        @block.tensor
        def _(pe):
            def turn_counts(saved, saved_n, done):
                pe.wait_ge(saved, saved_n)
                for s in range(NT):
                    r = rows_of(s)
                    last = nc.tensor.transpose(PSF[:r, TURN + s * P:TURN + (s + 1) * P], A_rows[:, s * P:s * P + r], ident[:, :])
                last.then_inc(done, 1)

            def slab_products(bank, t, k, first, last):
                r = rows_of(t)
                for m, (a, b) in enumerate(PRODUCTS):
                    ins = nc.tensor.matmul(PS[:r, bank, :], HT[:, a, k, t * P:t * P + r], W[:, k, b, :],
                                           start=first and m == 0, stop=last and m == 2)
                return ins

            def y1_products(i, k, first, last):
                (half, t), bank = divmod(i, NT), BR1 + i % Y1_BANKS
                if first:
                    pe.wait_ge(y1_freed, i + 1)
                    pe.wait_ge(ht_lo, t + 1)
                if t == 0:
                    pe.wait_ge(w_lo, half * KF + k + 1)
                ins = slab_products(bank, t, k, first, last)
                if last:
                    ins.then_inc(y1_done, 1)
                elif t == NT - 1:
                    ins.then_inc(w_used, 1)

            pe.wait_ge(setup, 4)
            units = [(i, k) for i in range(EARLY) for k in range(KF)]
            for t in range(NT):
                r = rows_of(t)
                pe.wait_ge(h_ready, t + 1)
                if t >= 2:
                    pe.wait_ge(ht_lo, t - 1)
                for k in range(KF):
                    c = 2 * (t % 2) * 512 + k * P
                    last = nc.tensor.transpose(PSF[:, c:c + r], hbuf[:r, t % 2, k * P:(k + 1) * P], ident[:r, :r])
                last.then_inc(h_turned, 1)
                if t == 2:
                    pe.wait_ge(sampled, 1)
                    nc.tensor.matmul(PS[0:1, 5, 0:NW], ones[:EP, :], samples[:, :], start=True, stop=True).then_inc(counted, 1)
                for i, k in units[max(0, t - 2) * 4:max(0, t - 1) * 4]:
                    y1_products(i, k, k == 0, k == KF - 1)
            for i, k in units[(NT - 2) * 4:]:
                y1_products(i, k, k == 0, k == KF - 1)
            pe.wait_ge(ht_lo, NT)

            for what, *rest in stage1_order():
                n, step = (rest + [None])[0], rest[1:]
                if what == "y1":
                    i, k = n, step[0]
                    if i == 2 * NT - 1:
                        y1_products(i, k, k == 5, k == 4)
                    else:
                        y1_products(i, k, k == 0, k == KF - 1)
                elif what == "turn":
                    if n:
                        pe.wait_ge(cols_ready, 2 * n + 1)
                    turn_counts(counts_saved, n + 1, turned)
                elif what == "count":
                    if step[0] == 0:
                        pe.wait_ge(dst_ready, n + 1)
                        if n:
                            pe.wait_ge(counts_saved, n)
                    i = step[0]
                    by_act = sum(m <= i for m in ACT_STEPS)
                    pe.wait_ge(src_ready, n * (WPT * ROW - len(ACT_STEPS)) + (i + 1) * WPT - by_act)
                    if i in ACT_STEPS:
                        pe.wait_ge(act_src_ready, n * len(ACT_STEPS) + by_act)
                    for c, (o_, w_) in enumerate(ACH):
                        for j in range(WPT):
                            ins = nc.tensor.matmul(PS[j * WIN:(j + 1) * WIN, c, 0:w_],
                                                   ONEHOT_DST[n % 2][:, j * ROW + i, :],
                                                   onehot_src[:, (i * WPT + j) % SLOTS, o_:o_ + w_],
                                                   start=i == 0, stop=i == ROW - 1)
                    ins.then_inc(src_free, WPT)
                else:
                    pe.wait_ge(check_ready, 1)
                    nc.tensor.matmul(PS[0:1, 0, 0:2], ones[:, :], check[:, :], start=True, stop=True).then_inc(check_summed, 1)

            pe.wait_ge(flags_ready, 1)
            redo = pe.value_load(flags[0:1, 0:1], min_val=0, max_val=1)
            wide = pe.value_load(flags[0:1, 1:2], min_val=0, max_val=1)
            with pe.If(redo != 0):
                pe.wait_ge(cols_ready, 2 * NT + 1)
                with pe.Fori(0, NT) as t:
                    pe.wait_ge(g_cols, t * 2 + 1)
                    pe.wait_ge(g_ready, t * EPP + 1)
                    for c, (o_, w_) in enumerate(ACH):
                        nc.tensor.matmul(PS[:, c, 0:w_], zeros[:EP, :], iota_f16[:EP, 0:w_], start=True, stop=False)
                    with pe.Fori(0, RPP) as r:
                        for q in range(ROW):
                            pe.wait_ge(g_ready, t * EPP + r * ROW + (q + 1))
                            for c, (o_, w_) in enumerate(ACH):
                                ins = nc.tensor.matmul(PS[:, c, 0:w_], any_dst[:EP, q % 2, :],
                                                       onehot_src[:EP, q % 2, o_:o_ + w_], start=False, stop=False)
                            ins.then_inc(g_free, 1)
                    for c, (o_, w_) in enumerate(ACH):
                        ins = nc.tensor.matmul(PS[:, c, 0:w_], zeros[:EP, :], iota_f16[:EP, 0:w_], start=False, stop=True)
                    ins.then_inc(g_counts, 1)
                    turn_counts(g_saved, t + 1, g_turned)
                pe.wait_ge(g_cols, 2 * NT + 1)
                pe.wait_ge(g_written, 32 * NT)

            pe.wait_ge(y1_freed, Y1_BANKS + 2 * NT)
            pe.wait_ge(cols_ready, 2 * NT + 1)

            def feature_tile(j, parity, dt):
                banks = CHBANK[parity]
                pe.wait_ge(h1_freed, j * 3 + 1)
                pe.wait_ge(wst_lo, j + 1)
                for k in range(KF):
                    for m, (a, b) in enumerate(PRODUCTS):
                        for c, (o_, w_) in enumerate(CH):
                            ins = nc.tensor.matmul(PS[:, banks[c], 0:w_], W_st[:, a, k, :], HT[:, b, k, o_:o_ + w_],
                                                   start=k == 0 and m == 0, stop=False)
                ins.then_inc(wst_used, 1)
                pe.wait_ge(yst_lo, j * 2 + 2)
                pe.wait_ge(at_written, 32 * NT)
                for s in range(NT):
                    r = rows_of(s)
                    for part in (HI, LO):
                        for c, (o_, w_) in enumerate(CH):
                            ins = nc.tensor.matmul(PS[:, banks[c], 0:w_], y_st[:r, part, s, :].bitcast(dt),
                                                   AT[:r, s, o_:o_ + w_].bitcast(dt),
                                                   start=False, stop=s == NT - 1 and part == LO)
                ins.then_inc(h1_done, 1)

            def layer_two(half, dt):
                for t in range(NT):
                    pe.wait_ge(tile_freed, half * (2 * NT) + (t + 1))
                    if t in (0, 3, 6):
                        pe.wait_ge(h1_lo, KF + t // 3)
                    for k in range(KF):
                        if t == 0:
                            pe.wait_ge(w_lo, half * (2 * KF) + (2 * KF + k + 1))
                        ins = slab_products(RING34[t % 4], t, k, k == 0, k == KF - 1)
                        if k == KF - 1:
                            ins.then_inc(tile_done, 1)
                        elif t == NT - 1:
                            ins.then_inc(w_used, 1)
                for t in range(NT):
                    bank = RING34[(NT + t) % 4]
                    pe.wait_ge(tile_freed, half * (2 * NT) + (NT + t + 1))
                    for k in range(KF):
                        if t == 0:
                            pe.wait_ge(w_lo, half * (2 * KF) + (3 * KF + k + 1))
                        ins = slab_products(bank, t, k, k == 0, False)
                        if t == NT - 1:
                            ins.then_inc(w_used, 1)
                    if t == 0:
                        pe.wait_ge(tile_freed, half * (2 * NT) + (4 + NT))
                    for s in range(NT):
                        r = rows_of(s)
                        for part in (HI, LO):
                            ins = nc.tensor.matmul(PS[:rows_of(t), bank, :], AT[:r, s, t * P:t * P + rows_of(t)].bitcast(dt),
                                                   y2[:r, s, part, :].bitcast(dt),
                                                   start=False, stop=s == NT - 1 and part == LO)
                    ins.then_inc(tile_done, 1)

            for want, dt in ((0, F32R), (1, F32)):
                with pe.If(wide == want):
                    with pe.Fori(0, KF // 2) as q:
                        for parity in range(2):
                            feature_tile(q * 2 + parity, parity, dt)
                    with pe.Fori(0, 2) as half:
                        layer_two(half, dt)


def kernel(x, src, dst, L0_gnn_Ws1, L0_gnn_Wn1, L0_gnn_b1, L0_gnn_Ws2, L0_gnn_Wn2, L0_gnn_b2):
    import numpy as np
    import concourse.bacc as bacc
    from concourse.bass_utils import run_bass_kernel_spmd

    nc = bacc.Bacc("TRN2", target_bir_lowering=False, num_devices=1)
    arrays, args = {}, []
    for name, a in (("x", x), ("src", src), ("dst", dst), ("ws1", L0_gnn_Ws1), ("wn1", L0_gnn_Wn1), ("b1", L0_gnn_b1),
                    ("ws2", L0_gnn_Ws2), ("wn2", L0_gnn_Wn2), ("b2", L0_gnn_b2)):
        a = np.ascontiguousarray(a)
        arrays[name + "_in"] = a
        args.append(nc.dram_tensor(name + "_in", a.shape, mybir.dt.from_np(a.dtype), kind="ExternalInput").ap())
    args.append(nc.dram_tensor("out_0", (N, D), F32, kind="ExternalOutput").ap())
    gnn_kernel(nc, *args)
    r = run_bass_kernel_spmd(nc, [arrays], core_ids=[0])
    return r.results[0]["out_0"]
```
